# Optimizing a Trainium2 kernel written in Bass

```python
import numpy as np
import jax
import jax.numpy as jnp

def _softmax(x, axis=-1):
    return jax.nn.softmax(x, axis=axis)

def _gelu(x):
    return jax.nn.gelu(x, approximate=True)

def _silu(x):
    return jax.nn.silu(x)

def _sigmoid(x):
    return jax.nn.sigmoid(x)

def _layernorm(x, axis=-1, eps=1e-05):
    m = jnp.mean(x, axis=axis, keepdims=True)
    v = jnp.var(x, axis=axis, keepdims=True)
    return (x - m) / jnp.sqrt(v + eps)

def _scatter_add(tgt, idx, src, axis=0):
    return tgt.at[idx].add(src)

def _segment_sum(src, seg, n):
    return jax.ops.segment_sum(src, seg, n)
kernel_name = 'mk_gnn_resnorm_d1_gnn_r32_fde743'

def setup_inputs(seed: int=0):
    np.random.seed(seed)
    _w = jnp.asarray

    def _rec_inputs():
        import jax
        import jax.numpy as jnp
        _gk = jax.random.key(seed)
        x = -0.0002928 + 1 * jax.random.normal(jax.random.fold_in(_gk, 1), (50000, 256), jnp.float32)
        src = jax.random.randint(jax.random.fold_in(_gk, 2), (25000,), 0, 50000, jnp.int32)
        dst = jnp.minimum((50000 * jax.random.uniform(jax.random.fold_in(_gk, 3), (25000,)) ** 2.0).astype(jnp.int32), 49999)
        _o = jnp.argsort(dst, stable=True)
        src = src[_o]
        dst = dst[_o]
        return (x, src, dst)
    x, src, dst = _rec_inputs()

    def _L0_gnn_setup():
        import jax, jax.numpy as jnp
        import numpy as np
        N_NODES = 512
        D_FEAT = 256
        N_EDGES = 8192
        HIDDEN = 512
        D_OUT = 256
        key = jax.random.key(seed)
        ks = jax.random.split(key, 5)
        x = jax.random.normal(ks[0], (N_NODES, D_FEAT), dtype=jnp.float32)
        W1 = jax.random.normal(ks[1], (2 * D_FEAT, HIDDEN), dtype=jnp.float32) * (1.0 / np.sqrt(2 * D_FEAT))
        b1 = jnp.zeros((HIDDEN,), dtype=jnp.float32)
        W2 = jax.random.normal(ks[2], (HIDDEN, D_OUT), dtype=jnp.float32) * (1.0 / np.sqrt(HIDDEN))
        b2 = jnp.zeros((D_OUT,), dtype=jnp.float32)
        nn_index = jax.random.randint(ks[3], (2, N_EDGES), 0, N_NODES, dtype=jnp.int64)
        return {'x': x, 'W1': W1, 'b1': b1, 'W2': W2, 'b2': b2, 'nn_index': nn_index, 'k': 16}
    _L0_gnn_all = _L0_gnn_setup()
    _L0_gnn_in = {k: v for k, v in _L0_gnn_all.items() if k in ('W1', 'b1', 'W2', 'b2')}
    del _L0_gnn_all
    return {'x': x, 'src': src, 'dst': dst, 'L0_gnn_W1': _L0_gnn_in['W1'], 'L0_gnn_b1': _L0_gnn_in['b1'], 'L0_gnn_W2': _L0_gnn_in['W2'], 'L0_gnn_b2': _L0_gnn_in['b2']}

def reference(x, src, dst, L0_gnn_W1, L0_gnn_b1, L0_gnn_W2, L0_gnn_b2):
    import jax
    import jax.numpy as jnp

    def _L0_gnn_ref(x, W1, b1, W2, b2, nn_index, k):
        import jax, jax.numpy as jnp
        import numpy as np
        N_NODES = 512
        D_FEAT = 256
        N_EDGES = 8192
        HIDDEN = 512
        D_OUT = 256
        num_nodes = x.shape[0]
        src = nn_index[0]
        tgt = nn_index[1]
        x_i = x[tgt]
        x_j = x[src]
        feat = jnp.concatenate([x_i, x_j - x_i], axis=-1)
        h = jax.nn.relu(feat @ W1 + b1)
        msg = h @ W2 + b2
        out = jax.ops.segment_sum(msg, tgt, num_segments=num_nodes)
        deg = jax.ops.segment_sum(jnp.ones((msg.shape[0], 1), dtype=msg.dtype), tgt, num_segments=num_nodes)
        return out / (deg + 1e-08)
    edge_index = jnp.stack([src, dst])
    x = _layernorm(x + _L0_gnn_ref(x, L0_gnn_W1, L0_gnn_b1, L0_gnn_W2, L0_gnn_b2, edge_index, 16), axis=-1)
    return x

_drawn_inputs = setup_inputs


def setup_inputs(seed=0):
    import zlib

    import numpy as np

    out = dict(_drawn_inputs(seed))
    spreads = {'L0_gnn_b1': (0.0, 0.267), 'L0_gnn_b2': (0.0, 0.1)}
    factors = {}
    for name, (base, spread) in spreads.items():
        noise = np.random.default_rng([zlib.crc32(name.encode()), seed]).standard_normal(out[name].shape)
        drawn = base * np.exp(spread * noise) if base else spread * noise
        out[name] = jnp.asarray(drawn.astype(out[name].dtype))
    for name, factor in factors.items():
        out[name] = (out[name] * factor).astype(out[name].dtype)
    return out
```

```python
from contextlib import ExitStack

import concourse.bass as bass
from concourse import mybir

F32 = mybir.dt.float32
F32R = mybir.dt.float32r
BF16 = mybir.dt.bfloat16
I32 = mybir.dt.int32
ALU = mybir.AluOpType
ACT = mybir.ActivationFunctionType
AX = mybir.AxisListType

P = 128
NODES = 50000
FEAT = 256
HIDDEN = 512
EDGES = 25000
TILES = 4
GROUP = TILES * P
GROUPS = -(-EDGES // GROUP)
LAST = GROUPS - 1
PAIRS = LAST // 2
EROW = 2 * P
EROWS = GROUPS * GROUP // EROW
FULL = EDGES // EROW
REST = EDGES - FULL * EROW
PAD = 60000
SKIP = 65536
KC = 2 * FEAT // P
HC = HIDDEN // P
MC = FEAT // P
EPS_DEG = 1e-8
EPS_LN = 1e-5

NODE_ROWS = 5
BLOCK = NODE_ROWS * P
BLOCKS = NODES // BLOCK
TAIL = NODES - BLOCKS * BLOCK
SLOTS = 4
ACT_ROWS = 3
PER_STEP = 4
FILL_END = 9
FIRST_BLOCKS = BLOCKS - FILL_END * 2 * PER_STEP
CATCH_END = 17
HOLD = 2 * FILL_END


def live(s):
    return not isinstance(s, int) or 0 <= s < GROUPS


def wait(eng, sem, value):
    if not isinstance(value, int) or value > 0:
        eng.wait_ge(sem, value)


def gnn_residual_layernorm(nc, x, src, dst, W1, b1, W2, b2, same_dram, carry_dram, out):
    with ExitStack() as ctx:
        def sb(name, shape, dt):
            return ctx.enter_context(nc.sbuf_tensor(name, shape, dt))

        def psum(name, shape):
            return ctx.enter_context(nc.psum_tensor(name, shape, F32))

        def sem(name):
            return ctx.enter_context(nc.semaphore(name))

        ident = sb("ident", [P, P], F32)
        w1_hi = sb("w1_hi", [P, KC, HIDDEN], F32R)
        w1_lo = sb("w1_lo", [P, KC, HIDDEN], F32R)
        w2_hi = sb("w2_hi", [P, HC, FEAT], F32R)
        w2_lo = sb("w2_lo", [P, HC, FEAT], F32R)
        b1_col = sb("b1_col", [P, HC], F32)
        b2_row = sb("b2_row", [P, FEAT], F32)
        eps = sb("eps", [P, 1], F32)
        hold = sb("hold", [P, HOLD, TILES, FEAT], F32)
        ends = sb("ends", [EROWS, 2], F32)
        ends_flat = sb("ends_flat", [1, 2, EROWS], F32)
        carry_flat = sb("carry_flat", [1, EROWS + 1], F32)
        carry = sb("carry", [EROWS, 1], F32)
        early = hold[:, HOLD - 6:HOLD - 3].rearrange("p a t f -> p (a t f)")

        def table(at, n, dt=F32):
            return early[0:EROWS, at * EROW:at * EROW + n].bitcast(dt)

        dst_int = table(0, EROW + 2, I32)
        src_int = table(2, EROW, I32)
        dst_row = table(3, EROW + 2)
        src_row = table(5, EROW)
        take_row = table(6, EROW)
        put_row = table(7, EROW)
        same_row = table(8, EROW)
        ones_row = table(9, EROW)
        deg_row = table(10, EROW)
        same_bf = table(11, EROW // 2, BF16)
        w1_raw = hold[:, HOLD - 2:HOLD].rearrange("p a t f -> p (a t f)").rearrange("p (k n) -> p k n", k=KC)
        w2_raw = hold[:, HOLD - 3].rearrange("p t f -> p (t f)").rearrange("p (c n) -> p c n", c=HC)
        tail = hold[0:TAIL, HOLD - 7, 0]
        take = sb("take", [P, GROUPS, 2 * TILES], I32)
        put = sb("put", [P, GROUPS, TILES], I32)
        inv_deg = sb("inv_deg", [P, GROUPS, TILES], F32)
        take_now = sb("take_now", [P, 2, 2 * TILES], I32)
        put_now = sb("put_now", [P, 2, TILES], I32)
        xi = sb("xi", [P, 2, TILES, FEAT], F32)
        xj = sb("xj", [P, 2, TILES, FEAT], F32)
        xt_hi = sb("xt_hi", [P, 2, KC, GROUP], F32R)
        xt_lo = sb("xt_lo", [P, 2, KC, GROUP], F32R)
        h = sb("h", [P, 2, GROUP], F32)
        h_hi = sb("h_hi", [P, HC, GROUP], F32R)
        h_lo = sb("h_lo", [P, HC, GROUP], F32R)
        same = sb("same", [P, 2, GROUP], BF16)
        sums = sb("sums", [P, MC, GROUP], F32)
        e_stats = sb("e_stats", [P, 2, TILES, 6], F32)
        e_mv = sb("e_mv", [P, 2, TILES, 2], F32)
        e_std = sb("e_std", [P, 2, TILES], F32)
        e_rstd = sb("e_rstd", [P, GROUPS, TILES], F32)
        e_shift = sb("e_shift", [P, GROUPS, TILES], F32)
        done_rows = sb("done_rows", [P, 2, TILES, FEAT], F32)
        node = sb("node", [P, SLOTS, NODE_ROWS, FEAT], F32)
        n_stats = sb("n_stats", [P, SLOTS, NODE_ROWS, 6], F32)
        n_mv = sb("n_mv", [P, SLOTS, NODE_ROWS, 2], F32)
        n_std = sb("n_std", [P, SLOTS, NODE_ROWS], F32)
        n_rstd = sb("n_rstd", [P, SLOTS, NODE_ROWS], F32)
        n_shift = sb("n_shift", [P, SLOTS, NODE_ROWS], F32)
        t_stats = sb("t_stats", [TAIL, 6], F32)
        t_mv = sb("t_mv", [TAIL, 2], F32)
        t_std = sb("t_std", [TAIL, 1], F32)
        t_rstd = sb("t_rstd", [TAIL, 1], F32)
        t_shift = sb("t_shift", [TAIL, 1], F32)

        turn = psum("turn", [P, 2, GROUP])
        l1 = psum("l1", [P, 2, GROUP])
        l2 = psum("l2", [P, 2, MC, GROUP])

        w_in, b1_in, b2_in = sem("w_in"), sem("b1_in"), sem("b2_in")
        pad_set = sem("pad_set")
        dst_in, src_in, edge_in = sem("dst_in"), sem("src_in"), sem("edge_in")
        ident_made = sem("ident_made")
        prep = sem("prep")
        rows_ready = sem("rows_ready")
        cols_turned = sem("cols_turned")
        cols_ready = sem("cols_ready")
        same_ready, same_out = sem("same_ready"), sem("same_out")
        ends_ready, ends_out, ends_in = sem("ends_ready"), sem("ends_out"), sem("ends_in")
        carry_ready, carry_out, carry_in = sem("carry_ready"), sem("carry_out"), sem("carry_in")
        w_diff, w_hi, w_lo = sem("w_diff"), sem("w_hi"), sem("w_lo")
        take_set, put_set = sem("take_set"), sem("put_set")
        xi_in = [sem(f"xi_in{p}") for p in range(2)]
        xj_in = [sem(f"xj_in{p}") for p in range(2)]
        same_in = [sem(f"same_in{p}") for p in range(2)]
        scattered = [sem(f"scattered{p}") for p in range(2)]
        xt_turned = sem("xt_turned")
        xt_hi_done, xt_lo_done = sem("xt_hi_done"), sem("xt_lo_done")
        residual = sem("residual")
        l1_done, l2_done = sem("l1_done"), sem("l2_done")
        h_done, h_hi_done, h_lo_done = sem("h_done"), sem("h_hi_done"), sem("h_lo_done")
        summed = sem("summed")
        turned_back = sem("turned_back")
        y_done = sem("y_done")
        e_bn = sem("e_bn")
        e_var = sem("e_var")
        e_root = sem("e_root")
        e_inv = sem("e_inv")
        e_ready = sem("e_ready")
        normed = sem("normed")
        node_in = [sem(f"node_in{i}") for i in range(SLOTS)]
        node_out = [sem(f"node_out{i}") for i in range(SLOTS)]
        n_bn = sem("n_bn")
        n_var = sem("n_var")
        n_root = sem("n_root")
        n_inv = sem("n_inv")
        n_ready = sem("n_ready")
        n_act, n_pool = sem("n_act"), sem("n_pool")
        tail_in, tail_var, tail_root, tail_ready = sem("tail_in"), sem("tail_var"), sem("tail_root"), sem("tail_ready")
        tail_chain, tail_done, tail_out = sem("tail_chain"), sem("tail_done"), sem("tail_out")

        def wait_alone(eng, sem, value):
            value = value if isinstance(value, int) else eng.to_reg(value)
            eng.wait_ge(ident_made, 2)
            eng.wait_ge(sem, value)

        def block_rows(t, b):
            return t[bass.ds(b * BLOCK, BLOCK), :].rearrange("(p r) f -> p r f", p=P)

        def fill_steps(eng, step):
            step(-1, 1, "fill")
            step(0, 0, "fill")
            step(1, 1, "fill")
            with eng.Fori(1, FILL_END) as i:
                step(2 * i, 0, "fill")
                step(2 * i + 1, 1, "fill")

        def scatter_steps(eng, step):
            with eng.Fori(FILL_END, CATCH_END) as i:
                step(2 * i, 0, "catch")
                step(2 * i + 1, 1, "catch")
            with eng.Fori(CATCH_END, PAIRS - 1) as i:
                step(2 * i, 0, "even")
                step(2 * i + 1, 1, "even")
            for u in range(LAST - 2, LAST + 2):
                step(u, u % 2, "even")

        def finished_groups(u, par, phase):
            if phase == "fill":
                return []
            if phase == "catch":
                return [(2 * u - 4 * FILL_END, 0), (2 * u - 4 * FILL_END + 1, 1)]
            return [(u - 2, par)]

        def step_blocks(u, phase):
            if phase != "fill" or (isinstance(u, int) and u < 0):
                return [None] * PER_STEP
            return [(FIRST_BLOCKS + PER_STEP * u + n, (FIRST_BLOCKS + n) % SLOTS,
                     u + (FIRST_BLOCKS + n) // SLOTS) for n in range(PER_STEP)]

        def first_blocks():
            return [(b, b % SLOTS, b // SLOTS) for b in range(FIRST_BLOCKS)]

        def before(blk):
            b, slot, visit = blk
            return (b - 1, slot - 1, visit) if slot else (b - 1, SLOTS - 1, visit - 1)

        LAST_BLOCK = (BLOCKS - 1, (BLOCKS - 1) % SLOTS, (BLOCKS - 1) // SLOTS)

        def landed(s, par, n):
            return (s - par) * (n // 2) + n

        block = ctx.enter_context(nc.Block())

        @block.sync
        def _(sp):
            def load_block(blk):
                b, slot, visit = blk
                wait(sp, node_out[slot], 16 * visit)
                sp.dma_start(node[:, slot], block_rows(x, b)).then_inc(node_in[slot], 16)

            def store_block(blk):
                b, slot, _ = blk
                sp.wait_ge(n_act, b + 1)
                sp.wait_ge(n_pool, b + 1)
                sp.dma_start(block_rows(out, b), node[:, slot]).then_inc(node_out[slot], 16)

            sp.wait_ge(pad_set, 3)
            sp.dma_start(dst_int[0:FULL, 1:EROW + 1],
                         dst[0:FULL * EROW].rearrange("(q e) -> q e", e=EROW)).then_inc(dst_in, 16)
            sp.dma_start(dst_int[FULL:EROWS, 1:REST + 1],
                         dst[FULL * EROW:EDGES].rearrange("(q e) -> q e", q=1)).then_inc(dst_in, 16)
            sp.dma_start(src_int[0:FULL, :],
                         src[0:FULL * EROW].rearrange("(q e) -> q e", e=EROW)).then_inc(src_in, 16)
            sp.dma_start(src_int[FULL:EROWS, 0:REST],
                         src[FULL * EROW:EDGES].rearrange("(q e) -> q e", q=1)).then_inc(src_in, 16)
            rows = dst[0:FULL * EROW].rearrange("(q e) -> q e", e=EROW)
            with nc.allow_non_contiguous_dma(reason="the edge before and the edge after each row"):
                sp.dma_start(dst_int[1:EROWS, 0:1], rows[:, EROW - 1:EROW]).then_inc(edge_in, 16)
                sp.dma_start(dst_int[0:FULL - 1, EROW + 1:EROW + 2], rows[1:FULL, 0:1]).then_inc(edge_in, 16)
                sp.dma_start(dst_int[FULL - 1:FULL, EROW + 1:EROW + 2],
                             dst[FULL * EROW:FULL * EROW + 1].rearrange("(q e) -> q e", q=1)).then_inc(edge_in, 16)
            sp.dma_start(w1_raw, W1.rearrange("(k p) n -> p k n", p=P)).then_inc(w_in, 16)
            sp.dma_start(w2_raw, W2.rearrange("(c p) n -> p c n", p=P)).then_inc(w_in, 16)
            sp.dma_start(tail[:, :], x[BLOCKS * BLOCK:NODES, :]).then_inc(tail_in, 16)
            for b in range(SLOTS - 1):
                load_block((b, b, 0))
            sp.wait_ge(same_ready, 1)
            sp.dma_start(same_dram.rearrange("(q e) -> q e", e=EROW), same_bf[:, :]).then_inc(same_out, 16)
            sp.wait_ge(ends_ready, 1)
            sp.dma_start(carry_dram[0:EROWS, :], ends[:, :]).then_inc(ends_out, 16)
            sp.wait_ge(ends_out, 16)
            with nc.allow_non_contiguous_dma(reason="196 values, once"):
                sp.dma_start(ends_flat[:, :, :], carry_dram[0:EROWS, :].rearrange("(o q) a -> o a q", o=1))\
                    .then_inc(ends_in, 16)
            sp.wait_ge(carry_ready, 1)
            sp.dma_start(carry_dram[EROWS:EROWS + EROWS // 2, :].rearrange("(o q) a -> o (q a)", o=1),
                         carry_flat[:, 0:EROWS]).then_inc(carry_out, 16)
            sp.wait_ge(carry_out, 16)
            sp.dma_start(carry[:, :], carry_dram[EROWS:EROWS + EROWS // 2, :]
                         .rearrange("q (a o) -> (q a) o", o=1)).then_inc(carry_in, 16)
            sp.wait_ge(same_out, 16)
            for blk in first_blocks():
                b = blk[0] + SLOTS - 1
                load_block((b, b % SLOTS, b // SLOTS))
                store_block(blk)
            sp.wait_ge(tail_done, 1)
            sp.dma_start(out[BLOCKS * BLOCK:NODES, :], tail[:, :]).then_inc(tail_out, 16)

            def step(u, par, phase, last_fill=False):
                if live(u):
                    wait(sp, summed, MC * (u - 2) + MC)
                    sp.dma_start(same[:, par], same_dram[bass.ds(u * GROUP, GROUP)].partition_broadcast(P))\
                        .then_inc(same_in[par], 16)
                for blk in step_blocks(u, phase):
                    if blk is not None:
                        b, slot, visit = blk
                        ahead = before((b + SLOTS, slot, visit + 1))
                        if not last_fill or blk[1] == (FIRST_BLOCKS) % SLOTS:
                            load_block(ahead)
                        store_block(blk)

            step(-1, 1, "fill")
            step(0, 0, "fill")
            step(1, 1, "fill")
            with sp.Fori(1, FILL_END - 1) as i:
                step(2 * i, 0, "fill")
                step(2 * i + 1, 1, "fill")
            step(2 * FILL_END - 2, 0, "fill")
            step(2 * FILL_END - 1, 1, "fill", last_fill=True)
            scatter_steps(sp, step)

        @block.gpsimd
        def _(pool):
            nc.gpsimd.memset(dst_int[:, :], PAD).then_inc(pad_set, 1)
            nc.gpsimd.memset(src_int[:, :], 0).then_inc(pad_set, 1)
            pool.wait_ge(pad_set, 2)
            nc.gpsimd.memset(dst_int[0:1, 0:1], -1).then_inc(pad_set, 1)
            nc.gpsimd.memset(ident[:, :], 0.0).then_inc(ident_made, 1)
            pool.wait_ge(ident_made, 1)
            nc.gpsimd.affine_select(out=ident[:, :], in_=ident[:, :], compare_op=ALU.not_equal, fill=1.0,
                                    base=0, pattern=[[-1, P]], channel_multiplier=1).then_inc(ident_made, 1)

            def normalise_rows(blk):
                b, slot, _ = blk
                wait_alone(pool, n_ready, b + 1)
                for r in range(ACT_ROWS, NODE_ROWS):
                    last = nc.gpsimd.tensor_scalar(node[:, slot, r], node[:, slot, r], n_rstd[:, slot, r:r + 1],
                                                   n_shift[:, slot, r:r + 1], ALU.mult, ALU.add)
                last.then_inc(n_pool, 1)

            def gather_start(s, par):
                wait(pool, xt_turned, KC * (s - 2) + KC)
                wait(pool, residual, (s - 2) + 1)
                nc.gpsimd.tensor_copy(take_now[:, par], take[:, bass.ds(s, 1)].rearrange("p a t -> p (a t)"))\
                    .then_inc(take_set, 1)
                wait_alone(pool, take_set, s + 1)

            def gather(par, t):
                for rows, col, landing in ((xi, TILES + t, xi_in), (xj, t, xj_in)):
                    nc.gpsimd.indirect_dma_start(
                        rows[:, par, t], None, x,
                        bass.IndirectOffsetOnAxis(ap=take_now[:, par, col:col + 1], axis=0))\
                        .then_inc(landing[par], 16)

            def scatter(s, par):
                wait(pool, scattered[par], (s - par) * 8 * TILES)
                nc.gpsimd.tensor_copy(put_now[:, par], put[:, bass.ds(s, 1)].rearrange("p a t -> p (a t)"))\
                    .then_inc(put_set, 1)
                pool.wait_ge(put_set, s + 1)
                for t in range(TILES):
                    wait_alone(pool, normed, TILES * s + t + 1)
                    nc.gpsimd.indirect_dma_start(
                        out, bass.IndirectOffsetOnAxis(ap=put_now[:, par, t:t + 1], axis=0),
                        done_rows[:, par, t], None, bounds_check=NODES - 1, oob_is_err=False)\
                        .then_inc(scattered[par], 16)

            pool.wait_ge(cols_ready, 2)
            gather_start(0, 0)
            for t in range(TILES):
                gather(0, t)
            for blk in first_blocks()[1:]:
                normalise_rows(before(blk))

            def step(u, par, phase):
                gathers = live(u + 2)
                if gathers:
                    gather_start(u + 2, par)
                for n, blk in enumerate(step_blocks(u, phase)):
                    if gathers:
                        gather(par, n)
                    if blk is not None:
                        normalise_rows(before(blk))
                for s, p in finished_groups(u, par, phase):
                    scatter(s, p)

            fill_steps(pool, step)
            normalise_rows(LAST_BLOCK)
            for slot in range(SLOTS):
                pool.wait_ge(node_out[slot], 16 * len(range(slot, BLOCKS, SLOTS)))
            pool.wait_ge(tail_out, 16)
            pool.wait_ge(cols_ready, 3)
            scatter_steps(pool, step)
            scatter(LAST, 0)
            pool.wait_ge(scattered[0], 16 * TILES * (LAST // 2 + 1))
            pool.wait_ge(scattered[1], 16 * TILES * (LAST // 2))

        @block.scalar
        def _(act):
            with nc.allow_non_contiguous_dma(reason="512 biases, once"):
                act.dma_start(b1_col[:, :], b1.rearrange("(c p) -> p c", p=P)).then_inc(b1_in, 16)
            act.dma_start(b2_row[:, :], b2.partition_broadcast(P)).then_inc(b2_in, 16)

            def root(blk):
                b, slot, _ = blk
                act.wait_ge(n_var, b + 1)
                nc.scalar.activation(n_std[:, slot], n_mv[:, slot, :, 1], ACT.Sqrt, bias=eps[:, :])\
                    .then_inc(n_root, 1)

            def normalise_rows(blk):
                b, slot, _ = blk
                act.wait_ge(n_ready, b + 1)
                for r in range(ACT_ROWS):
                    last = nc.scalar.activation(node[:, slot, r], node[:, slot, r], ACT.Identity,
                                                bias=n_shift[:, slot, r:r + 1], scale=n_rstd[:, slot, r:r + 1])
                last.then_inc(n_act, 1)

            act.wait_ge(w_diff, 1)
            nc.scalar.activation(w1_hi[:, :, :], w1_raw, ACT.Copy).then_inc(w_hi, 1)
            nc.scalar.activation(w2_hi[:, :, :], w2_raw, ACT.Copy).then_inc(w_hi, 1)
            act.wait_ge(tail_var, 1)
            nc.scalar.activation(t_std[:, :], t_mv[:, 1:2], ACT.Sqrt, bias=eps[0:TAIL, :]).then_inc(tail_root, 1)
            act.wait_ge(tail_ready, 1)
            nc.scalar.activation(tail[:, :], tail[:, :], ACT.Identity, bias=t_shift[:, :], scale=t_rstd[:, :])\
                .then_inc(tail_done, 1)
            for blk in first_blocks():
                root(blk)
                if blk[0]:
                    normalise_rows(before(blk))

            def split_x(s, par, k):
                act.wait_ge(xt_turned, KC * s + k + 1)
                wait(act, l1_done, HC * (s - 2) + HC)
                nc.scalar.activation(xt_hi[:, par, k], turn[:, (0, 1, 0, 0)[k]], ACT.Copy).then_inc(xt_hi_done, 1)

            def hidden(s, c):
                act.wait_ge(l1_done, HC * s + c + 1)
                wait(act, h_lo_done, HC * s + c - 1)
                nc.scalar.activation(h[:, c % 2], l1[:, c % 2], ACT.Relu, bias=b1_col[:, c:c + 1])\
                    .then_inc(h_done, 1)
                wait(act, l2_done, HC * (s - 1) + c + 1)
                nc.scalar.activation(h_hi[:, c], l1[:, c % 2], ACT.Relu, bias=b1_col[:, c:c + 1])\
                    .then_inc(h_hi_done, 1)

            def edge_root(s, par):
                act.wait_ge(e_var, s + 1)
                nc.scalar.activation(e_std[:, par], e_mv[:, par, :, 1], ACT.Sqrt, bias=eps[:, :])\
                    .then_inc(e_root, 1)

            def final_row(s, par, t):
                if t == 0:
                    act.wait_ge(e_ready, s + 1)
                    wait(act, scattered[par], (s - par) * 8 * TILES)
                slot = s % HOLD
                nc.scalar.activation(
                    done_rows[:, par, t], hold[:, bass.ds(slot, 1), t].rearrange("p a f -> p (a f)"), ACT.Identity,
                    bias=e_shift[:, bass.ds(s, 1), t:t + 1].rearrange("p a b -> p (a b)"),
                    scale=e_rstd[:, bass.ds(s, 1), t:t + 1].rearrange("p a b -> p (a b)")).then_inc(normed, 1)

            act.wait_ge(b1_in, 16)

            def step(u, par, phase):
                blocks = step_blocks(u, phase)
                final = [(s, p, t) for s, p in finished_groups(u, par, phase) for t in range(TILES)]
                share = {0: (0, 0, 0, 0), 4: (0, 1, 1, 2), 8: (2, 2, 2, 2)}[len(final)]
                for c in range(HC):
                    if live(u + 1):
                        split_x(u + 1, 1 - par, c)
                    if live(u):
                        hidden(u, c)
                    if c == 0 and live(u - 2):
                        edge_root(u - 2, par)
                    if blocks[c] is not None:
                        root(blocks[c])
                        normalise_rows(before(blocks[c]))
                    for _ in range(share[c]):
                        final_row(*final.pop(0))

            fill_steps(act, step)
            normalise_rows(LAST_BLOCK)
            scatter_steps(act, step)
            edge_root(LAST, 0)
            for t in range(TILES):
                final_row(LAST, 0, t)

        @block.tensor
        def _(pe):
            pe.wait_ge(ident_made, 2)
            for n, row in enumerate((src_row, take_row, put_row, deg_row)):
                pe.wait_ge(rows_ready, n + 1)
                for b in range(2):
                    last = nc.tensor.transpose(l2[:, n // 2, n % 2, b * EROWS:(b + 1) * EROWS],
                                               row[:, b * P:(b + 1) * P], ident[0:EROWS, 0:EROWS])
                last.then_inc(cols_turned, 1)

            def turn_x(s, par, k):
                if k == 0:
                    pe.wait_ge(xi_in[par], landed(s, par, 16 * TILES))
                    wait(pe, xt_lo_done, KC * s)
                elif k == 1:
                    wait(pe, y_done, 2 * s - 4)
                elif k == 2:
                    pe.wait_ge(xj_in[par], landed(s, par, 16 * TILES))
                    pe.wait_ge(xt_lo_done, KC * s + 1)
                else:
                    pe.wait_ge(xt_lo_done, KC * s + 3)
                rows = xi if k < 2 else xj
                for t in range(TILES):
                    last = nc.tensor.transpose(turn[:, (0, 1, 0, 0)[k], t * P:(t + 1) * P],
                                               rows[:, par, t, (k % 2) * P:(k % 2 + 1) * P], ident[:, :])
                last.then_inc(xt_turned, 1)

            def layer1(s, par, c):
                if c == 0:
                    pe.wait_ge(xt_lo_done, KC * s + KC)
                wait(pe, h_hi_done, HC * s + c - 1)
                cols = slice(c * P, (c + 1) * P)
                for k in range(KC):
                    nc.tensor.matmul(l1[:, c % 2], w1_hi[:, k, cols], xt_hi[:, par, k], start=(k == 0), stop=False)
                    nc.tensor.matmul(l1[:, c % 2], w1_hi[:, k, cols], xt_lo[:, par, k], start=False, stop=False)
                    last = nc.tensor.matmul(l1[:, c % 2], w1_lo[:, k, cols], xt_hi[:, par, k], start=False,
                                            stop=(k == KC - 1))
                last.then_inc(l1_done, 1)

            def layer2(s, par, c):
                pe.wait_ge(h_lo_done, HC * s + c + 1)
                if c == 0:
                    wait(pe, summed, MC * (s - 2) + MC)
                for m in range(MC):
                    cols = slice(m * P, (m + 1) * P)
                    nc.tensor.matmul(l2[:, par, m], w2_hi[:, c, cols], h_hi[:, c], start=(c == 0), stop=False)
                    nc.tensor.matmul(l2[:, par, m], w2_hi[:, c, cols], h_lo[:, c], start=False, stop=False)
                    last = nc.tensor.matmul(l2[:, par, m], w2_lo[:, c, cols], h_hi[:, c], start=False,
                                            stop=(c == HC - 1))
                last.then_inc(l2_done, 1)

            def turn_back(s, par, half, x_beside):
                if half == 0:
                    pe.wait_ge(summed, MC * s + MC)
                    if x_beside:
                        pe.wait_ge(xt_lo_done, KC * (s + 2) + 2)
                    wait(pe, y_done, 2 * s)
                else:
                    pe.wait_ge(y_done, 2 * s + 1)
                bank = turn[:, 1].rearrange("p (t f) -> p t f", f=FEAT)
                for t in range(2):
                    for m in range(MC):
                        at = (2 * half + t) * P
                        last = nc.tensor.transpose(bank[:, t, m * P:(m + 1) * P],
                                                   sums[:, m, at:at + P], ident[:, :])
                last.then_inc(turned_back, 1)

            def step(u, par, phase):
                if isinstance(u, int) and u == 0:
                    pe.wait_ge(w_lo, 2)
                    pe.wait_ge(cols_ready, 4)
                for c in range(HC):
                    if live(u + 1):
                        turn_x(u + 1, 1 - par, c)
                    if live(u):
                        layer1(u, par, c)
                    if c < 2 and live(u - 1):
                        layer2(u - 1, 1 - par, c + 2)
                    if c >= 2 and live(u):
                        layer2(u, par, c - 2)
                    if c >= 2 and live(u - 1):
                        turn_back(u - 1, 1 - par, c - 2, live(u + 1))

            fill_steps(pe, step)
            scatter_steps(pe, step)

        @block.vector
        def _(dve):
            chain = [0]

            def chained(instruction):
                chain[0] += 1
                instruction.then_inc(prep, 1)
                dve.wait_ge(prep, chain[0])

            nc.vector.memset(eps[:, :], EPS_LN)
            nc.vector.memset(ones_row[:, :], 1.0)
            chained(nc.vector.memset(carry_flat[:, :], 0.0))
            dve.wait_ge(src_in, 32)
            nc.vector.tensor_copy(src_row[:, :], src_int[:, :]).then_inc(rows_ready, 1)
            dve.wait_ge(dst_in, 32)
            dve.wait_ge(edge_in, 48)
            chained(nc.vector.tensor_copy(dst_row[:, :], dst_int[:, :]))
            here = dst_row[:, 1:EROW + 1]
            nc.vector.tensor_scalar(take_row[:, :], here, float(NODES - 1), None, ALU.min).then_inc(rows_ready, 1)
            chained(nc.vector.tensor_tensor(put_row[:, :], here, dst_row[:, 2:EROW + 2], ALU.is_equal))
            nc.vector.scalar_tensor_tensor(out=put_row[:, :], in0=put_row[:, :], scalar=float(SKIP), in1=here,
                                           op0=ALU.mult, op1=ALU.add).then_inc(rows_ready, 1)
            nc.vector.tensor_tensor(same_bf[:, :], here, dst_row[:, 0:EROW], ALU.is_equal).then_inc(same_ready, 1)
            chained(nc.vector.tensor_tensor(same_row[:, :], here, dst_row[:, 0:EROW], ALU.is_equal))

            def columns(n, target):
                dve.wait_ge(cols_turned, n + 1)
                for b in range(2):
                    last = nc.vector.tensor_copy(
                        target[:, :, b:TILES:2],
                        l2[:, n // 2, n % 2, b * EROWS:(b + 1) * EROWS].rearrange("p (s r) -> p s r", r=2))
                return last

            columns(0, take[:, :, 0:TILES]).then_inc(cols_ready, 1)
            columns(1, take[:, :, TILES:2 * TILES]).then_inc(cols_ready, 1)

            dve.wait_ge(w_in, 32)
            nc.vector.tensor_tensor(w1_raw[:, 0:2], w1_raw[:, 0:2], w1_raw[:, 2:4], ALU.subtract).then_inc(w_diff, 1)
            dve.wait_ge(w_diff, 1)

            chained(nc.vector.tensor_reduce(ends[:, 0:1], same_row[:, :], AX.X, ALU.min))
            chained(nc.vector.tensor_tensor_scan(deg_row[:, :], same_row[:, :], ones_row[:, :], 0.0,
                                                 ALU.mult, ALU.add))
            nc.vector.tensor_copy(ends[:, 1:2], deg_row[:, EROW - 1:EROW]).then_inc(ends_ready, 1)
            dve.wait_ge(w_hi, 1)
            nc.vector.tensor_tensor(w1_lo[:, :, :], w1_raw, w1_hi[:, :, :].bitcast(F32), ALU.subtract).then_inc(w_lo, 1)
            dve.wait_ge(w_hi, 2)
            nc.vector.tensor_tensor(w2_lo[:, :, :], w2_raw, w2_hi[:, :, :].bitcast(F32), ALU.subtract).then_inc(w_lo, 1)
            columns(2, put[:, :, :]).then_inc(cols_ready, 1)
            dve.wait_ge(ends_in, 16)
            nc.vector.tensor_tensor_scan(carry_flat[:, 1:EROWS + 1], ends_flat[:, 0], ends_flat[:, 1], 0.0,
                                         ALU.mult, ALU.add).then_inc(carry_ready, 1)

            dve.wait_ge(tail_in, 16)
            nc.vector.bn_stats(t_stats[:, :], tail[:, :]).then_inc(tail_chain, 1)
            dve.wait_ge(tail_chain, 1)
            nc.vector.bn_aggr(t_mv[:, :], t_stats[:, :]).then_inc(tail_var, 1)
            dve.wait_ge(tail_root, 1)
            nc.vector.reciprocal(t_rstd[:, :], t_std[:, :]).then_inc(tail_chain, 1)
            dve.wait_ge(tail_chain, 2)
            nc.vector.scalar_tensor_tensor(out=t_shift[:, :], in0=t_mv[:, 0:1], scalar=-1.0, in1=t_rstd[:, :],
                                           op0=ALU.mult, op1=ALU.mult).then_inc(tail_ready, 1)

            def block_stats(blk):
                b, slot, visit = blk
                dve.wait_ge(node_in[slot], 16 * (visit + 1))
                for r in range(NODE_ROWS):
                    last = nc.vector.bn_stats(n_stats[:, slot, r], node[:, slot, r])
                last.then_inc(n_bn, 1)
                wait_alone(dve, n_bn, b + 1)
                for r in range(NODE_ROWS):
                    last = nc.vector.bn_aggr(n_mv[:, slot, r], n_stats[:, slot, r])
                last.then_inc(n_var, 1)

            def block_scale(blk):
                b, slot, _ = blk
                dve.wait_ge(n_root, b + 1)
                nc.vector.reciprocal(n_rstd[:, slot], n_std[:, slot]).then_inc(n_inv, 1)
                dve.wait_ge(n_inv, b + 1)
                nc.vector.scalar_tensor_tensor(out=n_shift[:, slot], in0=n_mv[:, slot, :, 0], scalar=-1.0,
                                               in1=n_rstd[:, slot], op0=ALU.mult, op1=ALU.mult).then_inc(n_ready, 1)

            for blk in first_blocks():
                if blk[0]:
                    block_scale(before(blk))
                block_stats(blk)
                if blk[0] == 2:
                    dve.wait_ge(carry_in, 16)
                    chained(nc.vector.tensor_tensor_scan(deg_row[:, :], same_row[:, :], ones_row[:, :],
                                                         carry[:, 0:1], ALU.mult, ALU.add))
                    chained(nc.vector.tensor_scalar(deg_row[:, :], deg_row[:, :], EPS_DEG, None, ALU.add))
                    nc.vector.reciprocal(deg_row[:, :], deg_row[:, :]).then_inc(rows_ready, 1)
                    columns(3, inv_deg[:, :, :]).then_inc(cols_ready, 1)
            dve.wait_ge(b2_in, 16)

            def add_residual(s, par, reused):
                dve.wait_ge(xi_in[par], landed(s, par, 16 * TILES))
                if reused:
                    dve.wait_ge(normed, TILES * (s - HOLD) + TILES)
                slot = s % HOLD
                nc.vector.tensor_tensor(hold[:, bass.ds(slot, 1)].rearrange("p a t f -> p (a t) f"), xi[:, par],
                                        b2_row[:, :].unsqueeze(1).broadcast_to([P, TILES, FEAT]),
                                        ALU.add).then_inc(residual, 1)

            def split_x(s, par, k):
                dve.wait_ge(xt_hi_done, KC * s + k + 1)
                nc.vector.tensor_tensor(xt_lo[:, par, k], turn[:, (0, 1, 0, 0)[k]], xt_hi[:, par, k].bitcast(F32),
                                        ALU.subtract).then_inc(xt_lo_done, 1)

            def split_h(s, c):
                dve.wait_ge(h_hi_done, HC * s + c + 1)
                nc.vector.tensor_tensor(h_lo[:, c], h[:, c % 2], h_hi[:, c].bitcast(F32),
                                        ALU.subtract).then_inc(h_lo_done, 1)

            def segment_sums(s, par):
                dve.wait_ge(l2_done, HC * s + HC)
                dve.wait_ge(same_in[par], landed(s, par, 16))
                wait(dve, turned_back, 2 * s)
                for m in range(MC):
                    wait(dve, summed, MC * (s - 1) + m + 1)
                    first = isinstance(s, int) and s == 0
                    nc.vector.tensor_tensor_scan(
                        sums[:, m], same[:, par], l2[:, par, m],
                        0.0 if first else sums[:, m, GROUP - 1:GROUP], ALU.mult, ALU.add)\
                        .then_inc(summed, 1)

            def rows_before_norm(s, half):
                dve.wait_ge(turned_back, 2 * s + half + 1)
                dve.wait_ge(residual, s + 1)
                slot = s % HOLD
                bank = turn[:, 1].rearrange("p (t f) -> p t f", f=FEAT)
                for t in range(2):
                    tile = 2 * half + t
                    row = hold[:, bass.ds(slot, 1), tile].rearrange("p a f -> p (a f)")
                    last = nc.vector.scalar_tensor_tensor(
                        out=row, in0=bank[:, t],
                        scalar=inv_deg[:, bass.ds(s, 1), tile:tile + 1].rearrange("p a b -> p (a b)"),
                        in1=row, op0=ALU.mult, op1=ALU.add)
                last.then_inc(y_done, 1)

            def edge_stats(s, par):
                wait_alone(dve, y_done, 2 * s + 2)
                slot = s % HOLD
                for t in range(TILES):
                    last = nc.vector.bn_stats(e_stats[:, par, t],
                                              hold[:, bass.ds(slot, 1), t].rearrange("p a f -> p (a f)"))
                last.then_inc(e_bn, 1)
                wait_alone(dve, e_bn, s + 1)
                for t in range(TILES):
                    last = nc.vector.bn_aggr(e_mv[:, par, t], e_stats[:, par, t])
                last.then_inc(e_var, 1)

            def edge_scale(s, par):
                dve.wait_ge(e_root, s + 1)
                rstd = e_rstd[:, bass.ds(s, 1)].rearrange("p a t -> p (a t)")
                shift = e_shift[:, bass.ds(s, 1)].rearrange("p a t -> p (a t)")
                nc.vector.reciprocal(rstd, e_std[:, par]).then_inc(e_inv, 1)
                dve.wait_ge(e_inv, s + 1)
                nc.vector.scalar_tensor_tensor(out=shift, in0=e_mv[:, par, :, 0], scalar=-1.0, in1=rstd,
                                               op0=ALU.mult, op1=ALU.mult).then_inc(e_ready, 1)

            def step(u, par, phase):
                blocks = step_blocks(u, phase)
                for c in range(HC):
                    if live(u + 1):
                        split_x(u + 1, 1 - par, c)
                    if c == 0 and live(u):
                        add_residual(u, par, phase != "fill")
                    if c == 2 and live(u - 1):
                        segment_sums(u - 1, 1 - par)
                    if c == 3 and live(u - 1):
                        rows_before_norm(u - 1, 0)
                    if live(u):
                        split_h(u, c)
                    if c == 0 and live(u - 2):
                        edge_scale(u - 2, par)
                    if blocks[c] is not None:
                        block_scale(before(blocks[c]))
                        block_stats(blocks[c])
                if live(u - 1):
                    rows_before_norm(u - 1, 1)
                    edge_stats(u - 1, 1 - par)

            fill_steps(dve, step)
            block_scale(LAST_BLOCK)
            scatter_steps(dve, step)
            edge_scale(LAST, 0)


_INS = ["x", "src", "dst", "L0_gnn_W1", "L0_gnn_b1", "L0_gnn_W2", "L0_gnn_b2"]


def kernel(**inputs):
    import numpy as _np
    import concourse.bacc as _bacc
    from concourse import mybir as _mybir
    from concourse.bass_utils import run_bass_kernel_spmd as _run

    nc = _bacc.Bacc("TRN2", target_bir_lowering=False, num_devices=1)
    arrays, args = {}, []
    for name in _INS:
        a = _np.ascontiguousarray(inputs[name])
        arrays[f"in_{name}_dram"] = a
        args.append(nc.dram_tensor(f"in_{name}_dram", a.shape, _mybir.dt.from_np(a.dtype), kind="ExternalInput").ap())
    same_dram = nc.dram_tensor("same_dram", (GROUPS * GROUP,), BF16, kind="Internal").ap()
    carry_dram = nc.dram_tensor("carry_dram", (EROWS + EROWS // 2, 2), F32, kind="Internal").ap()
    out = nc.dram_tensor("out_0_dram", (NODES, FEAT), F32, kind="ExternalOutput").ap()
    gnn_residual_layernorm(nc, *args, same_dram, carry_dram, out)
    r = _run(nc, [arrays], core_ids=[0])
    return r.results[0]["out_0_dram"]
```

```python
from contextlib import ExitStack

import concourse.bass as bass
from concourse import mybir

F32 = mybir.dt.float32
F32R = mybir.dt.float32r
BF16 = mybir.dt.bfloat16
I32 = mybir.dt.int32
ALU = mybir.AluOpType
ACT = mybir.ActivationFunctionType
AX = mybir.AxisListType

P = 128
NODES = 50000
FEAT = 256
HIDDEN = 512
EDGES = 25000
TILES = 4
GROUP = TILES * P
GROUPS = -(-EDGES // GROUP)
LAST = GROUPS - 1
PAIRS = LAST // 2
EROW = 2 * P
EROWS = GROUPS * GROUP // EROW
FULL = EDGES // EROW
REST = EDGES - FULL * EROW
LAST_EDGES = EDGES - LAST * GROUP
PAD = 60000
SKIP = 65536
KC = 2 * FEAT // P
HC = HIDDEN // P
MC = FEAT // P
EPS_DEG = 1e-8
EPS_LN = 1e-5

NODE_ROWS = 4
BLOCK = NODE_ROWS * P
BLOCKS = NODES // BLOCK
TAIL = (NODES - BLOCKS * BLOCK) // NODE_ROWS
SLOTS = 5
ACT_ROWS = 3
PER_STEP = 5
SPREAD = (1, 2, 1, 1)
FILL_END = 9
FIRST_BLOCKS = BLOCKS - FILL_END * 2 * PER_STEP
AHEAD = 3
CATCH_END = 17
HOLD = 2 * FILL_END


def edges(s):
    return slice(0, LAST_EDGES if isinstance(s, int) and s == LAST else GROUP)


def live(s):
    return not isinstance(s, int) or 0 <= s < GROUPS


def wait(eng, sem, value):
    if not isinstance(value, int) or value > 0:
        eng.wait_ge(sem, value)


def gnn_residual_layernorm(nc, x, src, dst, W1, b1, W2, b2, same_dram, carry_dram, out):
    with ExitStack() as ctx:
        def sb(name, shape, dt):
            return ctx.enter_context(nc.sbuf_tensor(name, shape, dt))

        def psum(name, shape):
            return ctx.enter_context(nc.psum_tensor(name, shape, F32))

        def sem(name):
            return ctx.enter_context(nc.semaphore(name))

        ident = sb("ident", [P, P], F32)
        w1_hi = sb("w1_hi", [P, KC, HIDDEN], F32R)
        w1_lo = sb("w1_lo", [P, KC, HIDDEN], F32R)
        w2_hi = sb("w2_hi", [P, HC, FEAT], F32R)
        w2_lo = sb("w2_lo", [P, HC, FEAT], F32R)
        b1_col = sb("b1_col", [P, HC], F32)
        b2_row = sb("b2_row", [P, FEAT], F32)
        eps = sb("eps", [P, 1], F32)
        hold = sb("hold", [P, HOLD, TILES, FEAT], F32)
        ends = sb("ends", [EROWS, 2], F32)
        ends_flat = sb("ends_flat", [1, 2, EROWS], F32)
        carry_flat = sb("carry_flat", [1, EROWS + 1], F32)
        carry = sb("carry", [EROWS, 1], F32)
        early = hold[:, HOLD - 6:HOLD - 3].rearrange("p a t f -> p (a t f)")

        def table(at, n, dt=F32):
            return early[0:EROWS, at * EROW:at * EROW + n].bitcast(dt)

        dst_int = table(0, EROW + 2, I32)
        src_int = table(2, EROW, I32)
        dst_row = table(3, EROW + 2)
        src_row = table(5, EROW)
        take_row = table(6, EROW)
        put_row = table(7, EROW)
        same_row = table(8, EROW)
        ones_row = table(9, EROW)
        deg_row = table(10, EROW)
        same_bf = table(11, EROW // 2, BF16)
        w1_raw = hold[:, HOLD - 2:HOLD].rearrange("p a t f -> p (a t f)").rearrange("p (k n) -> p k n", k=KC)
        w2_raw = hold[:, HOLD - 3].rearrange("p t f -> p (t f)").rearrange("p (c n) -> p c n", c=HC)
        tail = hold[0:TAIL, HOLD - 7]
        take = sb("take", [P, GROUPS, 2 * TILES], I32)
        put = sb("put", [P, GROUPS, TILES], I32)
        inv_deg = sb("inv_deg", [P, GROUPS, TILES], F32)
        take_now = sb("take_now", [P, 2, 2 * TILES], I32)
        put_now = sb("put_now", [P, 2, TILES], I32)
        xi = sb("xi", [P, 2, TILES, FEAT], F32)
        xj = sb("xj", [P, 2, TILES, FEAT], F32)
        xt_hi = sb("xt_hi", [P, 2, KC, GROUP], F32R)
        xt_lo = sb("xt_lo", [P, 2, KC, GROUP], F32R)
        h = sb("h", [P, 2, GROUP], F32)
        h_hi = sb("h_hi", [P, HC, GROUP], F32R)
        h_lo = sb("h_lo", [P, HC, GROUP], F32R)
        same = sb("same", [P, 2, GROUP], BF16)
        sums = sb("sums", [P, MC, GROUP], F32)
        e_stats = sb("e_stats", [P, 2, TILES, 3], F32)
        e_std = sb("e_std", [P, 2, TILES], F32)
        e_rstd = sb("e_rstd", [P, GROUPS, TILES], F32)
        e_shift = sb("e_shift", [P, GROUPS, TILES], F32)
        done_rows = sb("done_rows", [P, 2, TILES, FEAT], F32)
        node = sb("node", [P, SLOTS, NODE_ROWS, FEAT], F32)
        n_stats = sb("n_stats", [P, SLOTS, NODE_ROWS, 3], F32)
        n_std = sb("n_std", [P, SLOTS, NODE_ROWS], F32)
        n_rstd = sb("n_rstd", [P, SLOTS, NODE_ROWS], F32)
        n_shift = sb("n_shift", [P, SLOTS, NODE_ROWS], F32)
        t_stats = sb("t_stats", [TAIL, NODE_ROWS, 3], F32)
        t_std = sb("t_std", [TAIL, NODE_ROWS], F32)
        t_rstd = sb("t_rstd", [TAIL, NODE_ROWS], F32)
        t_shift = sb("t_shift", [TAIL, NODE_ROWS], F32)

        turn = psum("turn", [P, 2, GROUP])
        l1 = psum("l1", [P, 2, GROUP])
        l2 = psum("l2", [P, 2, MC, GROUP])

        w_in, b1_in, b2_in = sem("w_in"), sem("b1_in"), sem("b2_in")
        pad_set = sem("pad_set")
        dst_in, src_in, edge_in = sem("dst_in"), sem("src_in"), sem("edge_in")
        ident_made = sem("ident_made")
        prep = sem("prep")
        rows_ready = sem("rows_ready")
        cols_turned = sem("cols_turned")
        cols_ready = sem("cols_ready")
        same_ready, same_out = sem("same_ready"), sem("same_out")
        ends_ready, ends_out, ends_in = sem("ends_ready"), sem("ends_out"), sem("ends_in")
        carry_ready, carry_out, carry_in = sem("carry_ready"), sem("carry_out"), sem("carry_in")
        w_diff, w_hi, w_lo = sem("w_diff"), sem("w_hi"), sem("w_lo")
        take_set, put_set = sem("take_set"), sem("put_set")
        xi_in = [sem(f"xi_in{p}") for p in range(2)]
        xj_in = [sem(f"xj_in{p}") for p in range(2)]
        same_in = [sem(f"same_in{p}") for p in range(2)]
        scattered = [sem(f"scattered{p}") for p in range(2)]
        xt_turned = sem("xt_turned")
        xt_hi_done, xt_lo_done = sem("xt_hi_done"), sem("xt_lo_done")
        residual = sem("residual")
        l1_done, l2_done = sem("l1_done"), sem("l2_done")
        h_done, h_hi_done, h_lo_done = sem("h_done"), sem("h_hi_done"), sem("h_lo_done")
        summed = sem("summed")
        turned_back = sem("turned_back")
        y_done = sem("y_done")
        e_var = sem("e_var")
        e_root = sem("e_root")
        e_inv = sem("e_inv")
        e_ready = sem("e_ready")
        normed = sem("normed")
        node_in = [sem(f"node_in{i}") for i in range(SLOTS)]
        node_out = [sem(f"node_out{i}") for i in range(SLOTS)]
        n_var = sem("n_var")
        n_root = sem("n_root")
        n_inv = sem("n_inv")
        n_ready = sem("n_ready")
        n_act, n_pool = sem("n_act"), sem("n_pool")
        tail_in, tail_var, tail_root, tail_ready = sem("tail_in"), sem("tail_var"), sem("tail_root"), sem("tail_ready")
        tail_chain, tail_done, tail_out = sem("tail_chain"), sem("tail_done"), sem("tail_out")

        def wait_alone(eng, sem, value):
            value = value if isinstance(value, int) else eng.to_reg(value)
            eng.wait_ge(ident_made, 2)
            eng.wait_ge(sem, value)

        def block_rows(t, b):
            return t[bass.ds(b * BLOCK, BLOCK), :].rearrange("(p r) f -> p r f", p=P)

        def fill_steps(eng, step, after_first=None, after_zero=None):
            step(-1, 1, "fill")
            if after_first:
                after_first()
            step(0, 0, "fill")
            if after_zero:
                after_zero()
            step(1, 1, "fill")
            with eng.Fori(1, FILL_END) as i:
                step(2 * i, 0, "fill")
                step(2 * i + 1, 1, "fill")

        def scatter_steps(eng, step):
            with eng.Fori(FILL_END, CATCH_END) as i:
                step(2 * i, 0, "catch")
                step(2 * i + 1, 1, "catch")
            with eng.Fori(CATCH_END, PAIRS - 1) as i:
                step(2 * i, 0, "even")
                step(2 * i + 1, 1, "even")
            for u in range(LAST - 2, LAST + 2):
                step(u, u % 2, "even")

        def finished_groups(u, par, phase):
            if phase == "fill":
                return []
            if phase == "catch":
                return [(2 * u - 4 * FILL_END, 0), (2 * u - 4 * FILL_END + 1, 1)]
            return [(u - 2, par)]

        def step_blocks(u, phase):
            if phase != "fill":
                return []
            if isinstance(u, int) and u < 0:
                return [(b, b % SLOTS, b // SLOTS) for b in range(AHEAD, FIRST_BLOCKS)]
            return [(FIRST_BLOCKS + PER_STEP * u + n, (FIRST_BLOCKS + n) % SLOTS,
                     u + (FIRST_BLOCKS + n) // SLOTS) for n in range(PER_STEP)]

        def parts(blocks):
            return [blocks[sum(SPREAD[:c]):sum(SPREAD[:c + 1])] for c in range(HC)]

        def ahead_blocks():
            return [(b, b % SLOTS, b // SLOTS) for b in range(AHEAD)]

        def before(blk):
            b, slot, visit = blk
            return (b - 1, slot - 1, visit) if slot else (b - 1, SLOTS - 1, visit - 1)

        LAST_BLOCK = (BLOCKS - 1, (BLOCKS - 1) % SLOTS, (BLOCKS - 1) // SLOTS)

        def landed(s, par, n):
            return (s - par) * (n // 2) + n

        block = ctx.enter_context(nc.Block())

        @block.sync
        def _(sp):
            def load_block(blk):
                b, slot, visit = blk
                wait(sp, node_out[slot], 16 * visit)
                sp.dma_start(node[:, slot], block_rows(x, b)).then_inc(node_in[slot], 16)

            def store_block(blk):
                b, slot, _ = blk
                by_act, by_pool = b + 1, b + 1 - AHEAD
                if not isinstance(b, int):
                    by_act, by_pool = sp.to_reg(by_act), sp.to_reg(by_pool)
                sp.wait_ge(n_act, by_act)
                wait(sp, n_pool, by_pool)
                sp.dma_start(block_rows(out, b), node[:, slot]).then_inc(node_out[slot], 16)

            sp.wait_ge(pad_set, 3)
            sp.dma_start(dst_int[0:FULL, 1:EROW + 1],
                         dst[0:FULL * EROW].rearrange("(q e) -> q e", e=EROW)).then_inc(dst_in, 16)
            sp.dma_start(dst_int[FULL:EROWS, 1:REST + 1],
                         dst[FULL * EROW:EDGES].rearrange("(q e) -> q e", q=1)).then_inc(dst_in, 16)
            sp.dma_start(src_int[0:FULL, :],
                         src[0:FULL * EROW].rearrange("(q e) -> q e", e=EROW)).then_inc(src_in, 16)
            sp.dma_start(src_int[FULL:EROWS, 0:REST],
                         src[FULL * EROW:EDGES].rearrange("(q e) -> q e", q=1)).then_inc(src_in, 16)
            rows = dst[0:FULL * EROW].rearrange("(q e) -> q e", e=EROW)
            with nc.allow_non_contiguous_dma(reason="the edge before and the edge after each row"):
                sp.dma_start(dst_int[1:EROWS, 0:1], rows[:, EROW - 1:EROW]).then_inc(edge_in, 16)
                sp.dma_start(dst_int[0:FULL - 1, EROW + 1:EROW + 2], rows[1:FULL, 0:1]).then_inc(edge_in, 16)
                sp.dma_start(dst_int[FULL - 1:FULL, EROW + 1:EROW + 2],
                             dst[FULL * EROW:FULL * EROW + 1].rearrange("(q e) -> q e", q=1)).then_inc(edge_in, 16)
            load_block((0, 0, 0))
            load_block((1, 1, 0))
            load_block((2, 2, 0))
            sp.dma_start(w1_raw, W1.rearrange("(k p) n -> p k n", p=P)).then_inc(w_in, 16)
            sp.dma_start(w2_raw, W2.rearrange("(c p) n -> p c n", p=P)).then_inc(w_in, 16)
            sp.dma_start(tail, x[BLOCKS * BLOCK:NODES, :].rearrange("(p r) f -> p r f", p=TAIL)).then_inc(tail_in, 16)
            for b in range(3, SLOTS - 1):
                load_block((b, b, 0))
            sp.wait_ge(same_ready, 1)
            sp.dma_start(same_dram.rearrange("(q e) -> q e", e=EROW), same_bf[:, :]).then_inc(same_out, 16)
            sp.wait_ge(ends_ready, 1)
            sp.dma_start(carry_dram[0:EROWS, :], ends[:, :]).then_inc(ends_out, 16)
            sp.wait_ge(ends_out, 16)
            with nc.allow_non_contiguous_dma(reason="196 values, once"):
                sp.dma_start(ends_flat[:, :, :], carry_dram[0:EROWS, :].rearrange("(o q) a -> o a q", o=1))\
                    .then_inc(ends_in, 16)
            def exchange_ahead(blk):
                b = blk[0] + SLOTS - 1
                store_block(blk)
                load_block((b, b % SLOTS, b // SLOTS))

            for blk in ahead_blocks()[:-1]:
                exchange_ahead(blk)
            sp.wait_ge(carry_ready, 1)
            sp.dma_start(carry_dram[EROWS:EROWS + EROWS // 2, :].rearrange("(o q) a -> o (q a)", o=1),
                         carry_flat[:, 0:EROWS]).then_inc(carry_out, 16)
            sp.wait_ge(carry_out, 16)
            sp.dma_start(carry[:, :], carry_dram[EROWS:EROWS + EROWS // 2, :]
                         .rearrange("q (a o) -> (q a) o", o=1)).then_inc(carry_in, 16)
            exchange_ahead(ahead_blocks()[-1])
            sp.wait_ge(same_out, 16)
            def step(u, par, phase, last_fill=False):
                if live(u):
                    wait(sp, summed, MC * (u - 2) + MC)
                    sp.dma_start(same[:, par], same_dram[bass.ds(u * GROUP, GROUP)].partition_broadcast(P))\
                        .then_inc(same_in[par], 16)
                for n, (b, slot, visit) in enumerate(step_blocks(u, phase)):
                    store_block((b, slot, visit))
                    if not last_fill or n == 0:
                        load_block(before((b + SLOTS, slot, visit + 1)))

            step(-1, 1, "fill")
            step(0, 0, "fill")
            sp.wait_ge(tail_done, 1)
            sp.dma_start(out[BLOCKS * BLOCK:NODES, :].rearrange("(p r) f -> p r f", p=TAIL), tail).then_inc(tail_out, 16)
            step(1, 1, "fill")
            with sp.Fori(1, FILL_END - 1) as i:
                step(2 * i, 0, "fill")
                step(2 * i + 1, 1, "fill")
            step(2 * FILL_END - 2, 0, "fill")
            step(2 * FILL_END - 1, 1, "fill", last_fill=True)
            scatter_steps(sp, step)

        @block.gpsimd
        def _(pool):
            nc.gpsimd.memset(dst_int[:, :], PAD).then_inc(pad_set, 1)
            nc.gpsimd.memset(src_int[:, :], 0).then_inc(pad_set, 1)
            pool.wait_ge(pad_set, 2)
            nc.gpsimd.memset(dst_int[0:1, 0:1], -1).then_inc(pad_set, 1)
            nc.gpsimd.memset(ident[:, :], 0.0).then_inc(ident_made, 1)
            pool.wait_ge(ident_made, 1)
            nc.gpsimd.affine_select(out=ident[:, :], in_=ident[:, :], compare_op=ALU.not_equal, fill=1.0,
                                    base=0, pattern=[[-1, P]], channel_multiplier=1).then_inc(ident_made, 1)

            def normalise_rows(blk):
                b, slot, _ = blk
                if isinstance(b, int) and b < AHEAD:
                    return
                wait_alone(pool, n_ready, b + 1)
                for r in range(ACT_ROWS, NODE_ROWS):
                    last = nc.gpsimd.tensor_scalar(node[:, slot, r], node[:, slot, r], n_rstd[:, slot, r:r + 1],
                                                   n_shift[:, slot, r:r + 1], ALU.mult, ALU.add)
                last.then_inc(n_pool, 1)

            def gather_start(s, par):
                wait(pool, xt_turned, KC * (s - 2) + KC)
                wait(pool, residual, (s - 2) + 1)
                nc.gpsimd.tensor_copy(take_now[:, par], take[:, bass.ds(s, 1)].rearrange("p a t -> p (a t)"))\
                    .then_inc(take_set, 1)
                wait_alone(pool, take_set, s + 1)

            def gather(par, part):
                rows, landing, first = (xi, xi_in, TILES) if part < 2 else (xj, xj_in, 0)
                for t in range(2 * (part % 2), 2 * (part % 2) + 2):
                    nc.gpsimd.indirect_dma_start(
                        rows[:, par, t], None, x,
                        bass.IndirectOffsetOnAxis(ap=take_now[:, par, first + t:first + t + 1], axis=0))\
                        .then_inc(landing[par], 16)

            def scatter(s, par):
                wait(pool, scattered[par], (s - par) * 8 * TILES)
                nc.gpsimd.tensor_copy(put_now[:, par], put[:, bass.ds(s, 1)].rearrange("p a t -> p (a t)"))\
                    .then_inc(put_set, 1)
                pool.wait_ge(put_set, s + 1)
                for t in range(TILES):
                    wait_alone(pool, normed, TILES * s + t + 1)
                    nc.gpsimd.indirect_dma_start(
                        out, bass.IndirectOffsetOnAxis(ap=put_now[:, par, t:t + 1], axis=0),
                        done_rows[:, par, t], None, bounds_check=NODES - 1, oob_is_err=False)\
                        .then_inc(scattered[par], 16)

            def add_residual(s, par):
                wait_alone(pool, xi_in[par], landed(s, par, 16 * TILES))
                nc.gpsimd.tensor_tensor(hold[:, bass.ds(s % HOLD, 1)].rearrange("p a t f -> p (a t) f"), xi[:, par],
                                        b2_row[:, :].unsqueeze(1).broadcast_to([P, TILES, FEAT]),
                                        ALU.add).then_inc(residual, 1)

            pool.wait_ge(cols_ready, 2)
            for s in range(2):
                gather_start(s, s)
                for part in range(HC):
                    gather(s, part)
            pool.wait_ge(b2_in, 16)

            def step(u, par, phase):
                gathers = live(u + 2) and not (isinstance(u, int) and u < 0)
                blocks = parts(step_blocks(u, phase))
                if phase == "fill" and live(u):
                    add_residual(u, par)
                if gathers:
                    gather_start(u + 2, par)
                for c in range(HC):
                    if gathers:
                        gather(par, c)
                    if phase == "fill":
                        for blk in blocks[c]:
                            normalise_rows(before(blk))
                for s, p in finished_groups(u, par, phase):
                    scatter(s, p)

            fill_steps(pool, step)
            normalise_rows(LAST_BLOCK)
            for slot in range(SLOTS):
                pool.wait_ge(node_out[slot], 16 * len(range(slot, BLOCKS, SLOTS)))
            pool.wait_ge(tail_out, 16)
            pool.wait_ge(cols_ready, 3)
            scatter_steps(pool, step)
            scatter(LAST, 0)
            pool.wait_ge(scattered[0], 16 * TILES * (LAST // 2 + 1))
            pool.wait_ge(scattered[1], 16 * TILES * (LAST // 2))

        @block.scalar
        def _(act):
            with nc.allow_non_contiguous_dma(reason="512 biases, once"):
                act.dma_start(b1_col[:, :], b1.rearrange("(c p) -> p c", p=P)).then_inc(b1_in, 16)
            act.dma_start(b2_row[:, :], b2.partition_broadcast(P)).then_inc(b2_in, 16)

            def root(blk):
                b, slot, _ = blk
                act.wait_ge(n_var, b + 1)
                nc.scalar.activation(n_std[:, slot], n_stats[:, slot, :, 2], ACT.Sqrt, bias=eps[:, :],
                                     scale=1.0 / FEAT)\
                    .then_inc(n_root, 1)

            def normalise_rows(blk):
                b, slot, _ = blk
                act.wait_ge(n_ready, b + 1)
                for r in range(NODE_ROWS if isinstance(b, int) and b < AHEAD else ACT_ROWS):
                    last = nc.scalar.activation(node[:, slot, r], node[:, slot, r], ACT.Identity,
                                                bias=n_shift[:, slot, r:r + 1], scale=n_rstd[:, slot, r:r + 1])
                last.then_inc(n_act, 1)

            def normalise_tail():
                act.wait_ge(tail_ready, 1)
                for n in range(NODE_ROWS):
                    last = nc.scalar.activation(tail[:, n], tail[:, n], ACT.Identity, bias=t_shift[:, n:n + 1],
                                                scale=t_rstd[:, n:n + 1])
                last.then_inc(tail_done, 1)

            root((0, 0, 0))
            for blk in ahead_blocks()[2:]:
                root(before(blk))
                normalise_rows(before(before(blk)))
            normalise_rows((AHEAD - 2, AHEAD - 2, 0))
            act.wait_ge(w_diff, 1)
            nc.scalar.activation(w1_hi[:, :, :], w1_raw, ACT.Copy).then_inc(w_hi, 1)
            nc.scalar.activation(w2_hi[:, :, :], w2_raw, ACT.Copy).then_inc(w_hi, 1)
            act.wait_ge(tail_var, 1)
            nc.scalar.activation(t_std[:, :], t_stats[:, :, 2], ACT.Sqrt, bias=eps[0:TAIL, :], scale=1.0 / FEAT)\
                .then_inc(tail_root, 1)

            def split_x(s, par, k):
                act.wait_ge(xt_turned, KC * s + k + 1)
                wait(act, l1_done, HC * (s - 2) + HC)
                nc.scalar.activation(xt_hi[:, par, k], turn[:, k % 2], ACT.Copy).then_inc(xt_hi_done, 1)

            def hidden(s, c):
                act.wait_ge(l1_done, HC * s + c + 1)
                wait(act, h_lo_done, HC * s + c - 1)
                nc.scalar.activation(h[:, c % 2], l1[:, c % 2], ACT.Relu, bias=b1_col[:, c:c + 1])\
                    .then_inc(h_done, 1)
                wait(act, l2_done, HC * (s - 1) + c + 1)
                nc.scalar.activation(h_hi[:, c], l1[:, c % 2], ACT.Relu, bias=b1_col[:, c:c + 1])\
                    .then_inc(h_hi_done, 1)

            def edge_root(s, par):
                act.wait_ge(e_var, s + 1)
                nc.scalar.activation(e_std[:, par], e_stats[:, par, :, 2], ACT.Sqrt, bias=eps[:, :],
                                     scale=1.0 / FEAT)\
                    .then_inc(e_root, 1)

            def final_row(s, par, t):
                if t == 0:
                    act.wait_ge(e_ready, s + 1)
                    wait(act, scattered[par], (s - par) * 8 * TILES)
                slot = s % HOLD
                nc.scalar.activation(
                    done_rows[:, par, t], hold[:, bass.ds(slot, 1), t].rearrange("p a f -> p (a f)"), ACT.Identity,
                    bias=e_shift[:, bass.ds(s, 1), t:t + 1].rearrange("p a b -> p (a b)"),
                    scale=e_rstd[:, bass.ds(s, 1), t:t + 1].rearrange("p a b -> p (a b)")).then_inc(normed, 1)

            act.wait_ge(b1_in, 16)

            def step(u, par, phase):
                blocks = parts(step_blocks(u, phase))
                final = [(s, p, t) for s, p in finished_groups(u, par, phase) for t in range(TILES)]
                share = {0: (0, 0, 0, 0), 4: (0, 1, 1, 2), 8: (2, 2, 2, 2)}[len(final)]
                if isinstance(u, int) and u < 0:
                    for c in range(HC):
                        split_x(0, 0, c)
                for c in range(HC):
                    if live(u + 1) and live(u):
                        split_x(u + 1, 1 - par, c)
                    for blk in blocks[c][:1]:
                        root(before(blk))
                    if c == 1 and live(u - 2):
                        edge_root(u - 2, par)
                    if live(u):
                        hidden(u, c)
                    for blk in blocks[c][:1]:
                        normalise_rows(before(blk))
                    for blk in blocks[c][1:]:
                        root(before(blk))
                        normalise_rows(before(blk))
                    for _ in range(share[c]):
                        final_row(*final.pop(0))

            fill_steps(act, step, after_zero=normalise_tail)
            root(LAST_BLOCK)
            normalise_rows(LAST_BLOCK)
            scatter_steps(act, step)
            edge_root(LAST, 0)
            for t in range(TILES):
                final_row(LAST, 0, t)

        @block.tensor
        def _(pe):
            pe.wait_ge(ident_made, 2)

            def turn_table(n, row):
                pe.wait_ge(rows_ready, n + 1)
                for b in range(2):
                    last = nc.tensor.transpose(l2[:, n // 2, n % 2, b * EROWS:(b + 1) * EROWS],
                                               row[:, b * P:(b + 1) * P], ident[0:EROWS, 0:EROWS])
                last.then_inc(cols_turned, 1)

            for n, row in enumerate((src_row, take_row, put_row)):
                turn_table(n, row)

            def turn_x(s, par, k):
                if k == 0:
                    pe.wait_ge(xi_in[par], landed(s, par, 16 * TILES))
                elif k == 2:
                    pe.wait_ge(xj_in[par], landed(s, par, 16 * TILES))
                wait(pe, xt_lo_done, KC * s + k - 1)
                rows = xi if k < 2 else xj
                for t in range(TILES):
                    last = nc.tensor.transpose(turn[:, k % 2, t * P:(t + 1) * P],
                                               rows[:, par, t, (k % 2) * P:(k % 2 + 1) * P], ident[:, :])
                last.then_inc(xt_turned, 1)

            def layer1(s, par, c):
                if c == 0:
                    pe.wait_ge(xt_lo_done, KC * s + KC)
                wait(pe, h_hi_done, HC * s + c - 1)
                cols, cut = slice(c * P, (c + 1) * P), edges(s)
                for k in range(KC):
                    nc.tensor.matmul(l1[:, c % 2, cut], w1_hi[:, k, cols], xt_hi[:, par, k, cut],
                                     start=(k == 0), stop=False)
                    nc.tensor.matmul(l1[:, c % 2, cut], w1_hi[:, k, cols], xt_lo[:, par, k, cut],
                                     start=False, stop=False)
                    last = nc.tensor.matmul(l1[:, c % 2, cut], w1_lo[:, k, cols], xt_hi[:, par, k, cut], start=False,
                                            stop=(k == KC - 1))
                last.then_inc(l1_done, 1)

            def layer2(s, par, c):
                pe.wait_ge(h_lo_done, HC * s + c + 1)
                if c == 0:
                    wait(pe, y_done, 2 * (s - 2) + 2)
                for m in range(MC):
                    cols, cut = slice(m * P, (m + 1) * P), edges(s)
                    nc.tensor.matmul(l2[:, par, m, cut], w2_hi[:, c, cols], h_hi[:, c, cut], start=(c == 0), stop=False)
                    nc.tensor.matmul(l2[:, par, m, cut], w2_hi[:, c, cols], h_lo[:, c, cut], start=False, stop=False)
                    last = nc.tensor.matmul(l2[:, par, m, cut], w2_lo[:, c, cols], h_hi[:, c, cut], start=False,
                                            stop=(c == HC - 1))
                last.then_inc(l2_done, 1)

            def turn_back(s, par, half):
                if half == 0:
                    pe.wait_ge(summed, MC * s + MC)
                bank = l2[:, par, half].rearrange("p (t f) -> p t f", f=FEAT)
                for t in range(2):
                    for m in range(MC):
                        at = (2 * half + t) * P
                        last = nc.tensor.transpose(bank[:, t, m * P:(m + 1) * P],
                                                   sums[:, m, at:at + P], ident[:, :])
                last.then_inc(turned_back, 1)

            def step(u, par, phase):
                if isinstance(u, int) and u == 0:
                    pe.wait_ge(w_lo, 2)
                    pe.wait_ge(cols_ready, 3)
                if isinstance(u, int) and u == 1:
                    pe.wait_ge(cols_ready, 4)
                for c in range(HC):
                    if live(u + 1):
                        turn_x(u + 1, 1 - par, c)
                    if live(u):
                        layer1(u, par, c)
                    if c < 2 and live(u - 1):
                        layer2(u - 1, 1 - par, c + 2)
                    if c == 3 and live(u - 1):
                        turn_back(u - 1, 1 - par, 0)
                        turn_back(u - 1, 1 - par, 1)
                    if c >= 2 and live(u):
                        layer2(u, par, c - 2)

            fill_steps(pe, step, after_zero=lambda: turn_table(3, deg_row))
            scatter_steps(pe, step)

        @block.vector
        def _(dve):
            chain = [0]

            def chained(instruction):
                chain[0] += 1
                instruction.then_inc(prep, 1)
                dve.wait_ge(prep, chain[0])

            nc.vector.memset(eps[:, :], EPS_LN)
            nc.vector.memset(ones_row[:, :], 1.0)
            chained(nc.vector.memset(carry_flat[:, :], 0.0))
            dve.wait_ge(src_in, 32)
            nc.vector.tensor_copy(src_row[:, :], src_int[:, :]).then_inc(rows_ready, 1)
            dve.wait_ge(dst_in, 32)
            dve.wait_ge(edge_in, 48)
            chained(nc.vector.tensor_copy(dst_row[:, :], dst_int[:, :]))
            here = dst_row[:, 1:EROW + 1]
            nc.vector.tensor_scalar(take_row[:, :], here, float(NODES - 1), None, ALU.min).then_inc(rows_ready, 1)
            chained(nc.vector.tensor_tensor(put_row[:, :], here, dst_row[:, 2:EROW + 2], ALU.is_equal))
            nc.vector.scalar_tensor_tensor(out=put_row[:, :], in0=put_row[:, :], scalar=float(SKIP), in1=here,
                                           op0=ALU.mult, op1=ALU.add).then_inc(rows_ready, 1)
            nc.vector.tensor_tensor(same_bf[:, :], here, dst_row[:, 0:EROW], ALU.is_equal).then_inc(same_ready, 1)
            chained(nc.vector.tensor_tensor(same_row[:, :], here, dst_row[:, 0:EROW], ALU.is_equal))

            def columns(n, target):
                dve.wait_ge(cols_turned, n + 1)
                for b in range(2):
                    last = nc.vector.tensor_copy(
                        target[:, :, b:TILES:2],
                        l2[:, n // 2, n % 2, b * EROWS:(b + 1) * EROWS].rearrange("p (s r) -> p s r", r=2))
                return last

            columns(0, take[:, :, 0:TILES]).then_inc(cols_ready, 1)
            columns(1, take[:, :, TILES:2 * TILES]).then_inc(cols_ready, 1)

            def pair_stats(target, rows):
                return nc.vector.bn_stats(target.rearrange("p r s -> p (r s)"), rows.rearrange("p r f -> p f r"))

            def block_stats(blk):
                b, slot, visit = blk
                dve.wait_ge(node_in[slot], 16 * (visit + 1))
                for n in range(0, NODE_ROWS, 2):
                    last = pair_stats(n_stats[:, slot, n:n + 2], node[:, slot, n:n + 2])
                last.then_inc(n_var, 1)

            def block_scale(blk):
                b, slot, _ = blk
                dve.wait_ge(n_root, b + 1)
                nc.vector.reciprocal(n_rstd[:, slot], n_std[:, slot]).then_inc(n_inv, 1)
                dve.wait_ge(n_inv, b + 1)
                nc.vector.scalar_tensor_tensor(out=n_shift[:, slot], in0=n_stats[:, slot, :, 1], scalar=-1.0,
                                               in1=n_rstd[:, slot], op0=ALU.mult, op1=ALU.mult).then_inc(n_ready, 1)

            for blk in ahead_blocks():
                block_stats(blk)
                if blk[0]:
                    block_scale(before(blk))

            def split_x(s, par, k):
                dve.wait_ge(xt_hi_done, KC * s + k + 1)
                nc.vector.tensor_tensor(xt_lo[:, par, k], turn[:, k % 2], xt_hi[:, par, k].bitcast(F32),
                                        ALU.subtract).then_inc(xt_lo_done, 1)

            chained(nc.vector.tensor_reduce(ends[:, 0:1], same_row[:, :], AX.X, ALU.min))
            chained(nc.vector.tensor_tensor_scan(deg_row[:, :], same_row[:, :], ones_row[:, :], 0.0,
                                                 ALU.mult, ALU.add))
            nc.vector.tensor_copy(ends[:, 1:2], deg_row[:, EROW - 1:EROW]).then_inc(ends_ready, 1)
            dve.wait_ge(w_in, 32)
            nc.vector.tensor_tensor(w1_raw[:, 0:2], w1_raw[:, 0:2], w1_raw[:, 2:4], ALU.subtract).then_inc(w_diff, 1)
            dve.wait_ge(w_diff, 1)
            columns(2, put[:, :, :]).then_inc(cols_ready, 1)
            dve.wait_ge(tail_in, 16)
            for n in range(0, NODE_ROWS, 2):
                last = pair_stats(t_stats[:, n:n + 2], tail[:, n:n + 2])
            last.then_inc(tail_var, 1)
            dve.wait_ge(w_hi, 1)
            nc.vector.tensor_tensor(w1_lo[:, :, :], w1_raw, w1_hi[:, :, :].bitcast(F32), ALU.subtract).then_inc(w_lo, 1)
            split_x(0, 0, 0)
            split_x(0, 0, 1)
            dve.wait_ge(w_hi, 2)
            nc.vector.tensor_tensor(w2_lo[:, :, :], w2_raw, w2_hi[:, :, :].bitcast(F32), ALU.subtract).then_inc(w_lo, 1)
            split_x(0, 0, 2)
            split_x(0, 0, 3)
            dve.wait_ge(ends_in, 16)
            nc.vector.tensor_tensor_scan(carry_flat[:, 1:EROWS + 1], ends_flat[:, 0], ends_flat[:, 1], 0.0,
                                         ALU.mult, ALU.add).then_inc(carry_ready, 1)
            dve.wait_ge(tail_root, 1)
            nc.vector.reciprocal(t_rstd[:, :], t_std[:, :]).then_inc(tail_chain, 1)
            dve.wait_ge(tail_chain, 1)
            nc.vector.scalar_tensor_tensor(out=t_shift[:, :], in0=t_stats[:, :, 1], scalar=-1.0, in1=t_rstd[:, :],
                                           op0=ALU.mult, op1=ALU.mult).then_inc(tail_ready, 1)

            def count_degrees():
                dve.wait_ge(carry_in, 16)
                chained(nc.vector.tensor_tensor_scan(deg_row[:, :], same_row[:, :], ones_row[:, :],
                                                     carry[:, 0:1], ALU.mult, ALU.add))
                chained(nc.vector.tensor_scalar(deg_row[:, :], deg_row[:, :], EPS_DEG, None, ALU.add))
                nc.vector.reciprocal(deg_row[:, :], deg_row[:, :]).then_inc(rows_ready, 1)

            def add_residual(s, par):
                dve.wait_ge(xi_in[par], landed(s, par, 16 * TILES))
                dve.wait_ge(normed, TILES * (s - HOLD) + TILES)
                slot = s % HOLD
                nc.vector.tensor_tensor(hold[:, bass.ds(slot, 1)].rearrange("p a t f -> p (a t) f"), xi[:, par],
                                        b2_row[:, :].unsqueeze(1).broadcast_to([P, TILES, FEAT]),
                                        ALU.add).then_inc(residual, 1)

            def split_h(s, c):
                dve.wait_ge(h_hi_done, HC * s + c + 1)
                nc.vector.tensor_tensor(h_lo[:, c], h[:, c % 2], h_hi[:, c].bitcast(F32),
                                        ALU.subtract).then_inc(h_lo_done, 1)

            def segment_sums(s, par):
                dve.wait_ge(l2_done, HC * s + HC)
                dve.wait_ge(same_in[par], landed(s, par, 16))
                wait(dve, turned_back, 2 * s)
                for m in range(MC):
                    wait(dve, summed, MC * (s - 1) + m + 1)
                    first = isinstance(s, int) and s == 0
                    nc.vector.tensor_tensor_scan(
                        sums[:, m], same[:, par], l2[:, par, m],
                        0.0 if first else sums[:, m, GROUP - 1:GROUP], ALU.mult, ALU.add)\
                        .then_inc(summed, 1)

            def rows_before_norm(s, par, half):
                dve.wait_ge(turned_back, 2 * s + half + 1)
                dve.wait_ge(residual, s + 1)
                slot = s % HOLD
                bank = l2[:, par, half].rearrange("p (t f) -> p t f", f=FEAT)
                for t in range(2):
                    tile = 2 * half + t
                    row = hold[:, bass.ds(slot, 1), tile].rearrange("p a f -> p (a f)")
                    last = nc.vector.scalar_tensor_tensor(
                        out=row, in0=bank[:, t],
                        scalar=inv_deg[:, bass.ds(s, 1), tile:tile + 1].rearrange("p a b -> p (a b)"),
                        in1=row, op0=ALU.mult, op1=ALU.add)
                last.then_inc(y_done, 1)

            def edge_stats(s, par):
                wait_alone(dve, y_done, 2 * s + 2)
                rows = hold[:, bass.ds(s % HOLD, 1)].rearrange("p a t f -> p (a t) f")
                for t in range(0, TILES, 2):
                    last = pair_stats(e_stats[:, par, t:t + 2], rows[:, t:t + 2])
                last.then_inc(e_var, 1)

            def edge_scale(s, par):
                dve.wait_ge(e_root, s + 1)
                rstd = e_rstd[:, bass.ds(s, 1)].rearrange("p a t -> p (a t)")
                shift = e_shift[:, bass.ds(s, 1)].rearrange("p a t -> p (a t)")
                nc.vector.reciprocal(rstd, e_std[:, par]).then_inc(e_inv, 1)
                dve.wait_ge(e_inv, s + 1)
                nc.vector.scalar_tensor_tensor(out=shift, in0=e_stats[:, par, :, 1], scalar=-1.0, in1=rstd,
                                               op0=ALU.mult, op1=ALU.mult).then_inc(e_ready, 1)

            def step(u, par, phase):
                blocks = parts(step_blocks(u, phase))
                for c in range(HC):
                    if c == 2 and live(u - 1):
                        segment_sums(u - 1, 1 - par)
                    if live(u + 1) and live(u):
                        split_x(u + 1, 1 - par, c)
                    for blk in blocks[c][:1]:
                        block_scale(before(blk))
                    if c == 1 and live(u - 2):
                        edge_scale(u - 2, par)
                    if c == 0 and phase != "fill" and live(u):
                        add_residual(u, par)
                    if live(u):
                        split_h(u, c)
                    for blk in blocks[c][:1]:
                        block_stats(blk)
                    for blk in blocks[c][1:]:
                        block_scale(before(blk))
                        block_stats(blk)
                    if isinstance(u, int) and u < 0 and c == 1:
                        count_degrees()
                if live(u - 1):
                    rows_before_norm(u - 1, 1 - par, 0)
                    rows_before_norm(u - 1, 1 - par, 1)
                    edge_stats(u - 1, 1 - par)

            def finish_degrees():
                columns(3, inv_deg[:, :, :]).then_inc(cols_ready, 1)

            fill_steps(dve, step, after_zero=finish_degrees)
            block_scale(LAST_BLOCK)
            dve.wait_ge(residual, 2 * FILL_END)
            scatter_steps(dve, step)
            edge_scale(LAST, 0)


_INS = ["x", "src", "dst", "L0_gnn_W1", "L0_gnn_b1", "L0_gnn_W2", "L0_gnn_b2"]


def kernel(**inputs):
    import numpy as _np
    import concourse.bacc as _bacc
    from concourse import mybir as _mybir
    from concourse.bass_utils import run_bass_kernel_spmd as _run

    nc = _bacc.Bacc("TRN2", target_bir_lowering=False, num_devices=1)
    arrays, args = {}, []
    for name in _INS:
        a = _np.ascontiguousarray(inputs[name])
        arrays[f"in_{name}_dram"] = a
        args.append(nc.dram_tensor(f"in_{name}_dram", a.shape, _mybir.dt.from_np(a.dtype), kind="ExternalInput").ap())
    same_dram = nc.dram_tensor("same_dram", (GROUPS * GROUP,), BF16, kind="Internal").ap()
    carry_dram = nc.dram_tensor("carry_dram", (EROWS + EROWS // 2, 2), F32, kind="Internal").ap()
    out = nc.dram_tensor("out_0_dram", (NODES, FEAT), F32, kind="ExternalOutput").ap()
    gnn_residual_layernorm(nc, *args, same_dram, carry_dram, out)
    r = _run(nc, [arrays], core_ids=[0])
    return r.results[0]["out_0_dram"]
```
